# Optimizing a Trainium2 kernel written in Bass

```python
import numpy as np
import jax
import jax.numpy as jnp

def _softmax(x, axis=-1):
    return jax.nn.softmax(x, axis=axis)

def _gelu(x):
    return jax.nn.gelu(x, approximate=True)

def _silu(x):
    return jax.nn.silu(x)

def _sigmoid(x):
    return jax.nn.sigmoid(x)

def _layernorm(x, axis=-1, eps=1e-05):
    m = jnp.mean(x, axis=axis, keepdims=True)
    v = jnp.var(x, axis=axis, keepdims=True)
    return (x - m) / jnp.sqrt(v + eps)

def _scatter_add(tgt, idx, src, axis=0):
    return tgt.at[idx].add(src)

def _segment_sum(src, seg, n):
    return jax.ops.segment_sum(src, seg, n)
kernel_name = 'mk_gnn_preln_d2_gnn_r64_18a7e2'

def setup_inputs(seed: int=0):
    np.random.seed(seed)
    _w = jnp.asarray

    def _rec_inputs():
        import jax
        import jax.numpy as jnp
        _gk = jax.random.key(seed)
        x = -0.0003713 + 1 * jax.random.normal(jax.random.fold_in(_gk, 1), (100000, 128), jnp.float32)
        src = jax.random.randint(jax.random.fold_in(_gk, 2), (50000,), 0, 100000, jnp.int32)
        dst = jax.random.randint(jax.random.fold_in(_gk, 3), (50000,), 0, 100000, jnp.int32)
        _o = jnp.argsort(dst, stable=True)
        src = src[_o]
        dst = dst[_o]
        return (x, src, dst)
    x, src, dst = _rec_inputs()

    def _L0_gnn_setup():
        import jax, jax.numpy as jnp
        import numpy as np
        N_NODES = 100000
        N_EDGES = 25000
        IN_C, HID_C, OUT_C = (128, 256, 128)
        EPS = 0.0

        def _gin_conv(x, src, dst, mlp):
            agg = jax.ops.segment_sum(x[src], dst, num_segments=N_NODES)
            h = (1.0 + EPS) * x + agg
            return mlp(h)
        key = jax.random.key(seed)
        ks = jax.random.split(key, 10)
        x = jax.random.normal(ks[0], (N_NODES, IN_C), dtype=jnp.float32)
        edge_index = jax.random.randint(ks[1], (2, N_EDGES), 0, N_NODES, dtype=jnp.int64)

        def lin(k, fan_in, fan_out):
            kw, kb = jax.random.split(k)
            bound = 1.0 / np.sqrt(fan_in)
            w = jax.random.uniform(kw, (fan_in, fan_out), minval=-bound, maxval=bound, dtype=jnp.float32)
            b = jax.random.uniform(kb, (fan_out,), minval=-bound, maxval=bound, dtype=jnp.float32)
            return (w, b)
        w1, b1 = lin(ks[2], IN_C, HID_C)
        w2, b2 = lin(ks[3], HID_C, HID_C)
        w3, b3 = lin(ks[4], HID_C, HID_C)
        w4, b4 = lin(ks[5], HID_C, OUT_C)
        return {'x': x, 'edge_index': edge_index, 'w1': w1, 'b1': b1, 'w2': w2, 'b2': b2, 'w3': w3, 'b3': b3, 'w4': w4, 'b4': b4}
    _L0_gnn_all = _L0_gnn_setup()
    _L0_gnn_in = {k: v for k, v in _L0_gnn_all.items() if k in ('w1', 'b1', 'w2', 'b2', 'w3', 'b3', 'w4', 'b4')}
    del _L0_gnn_all

    def _L1_gnn_setup():
        import jax, jax.numpy as jnp
        import numpy as np
        N_NODES = 100000
        N_EDGES = 25000
        IN_F, HID_F, OUT_F = (128, 256, 128)

        def _sage_conv(x, src, dst, W_self, W_neigh, b):
            msgs = x[src]
            summed = jax.ops.segment_sum(msgs, dst, num_segments=N_NODES)
            deg = jax.ops.segment_sum(jnp.ones((src.shape[0],), x.dtype), dst, num_segments=N_NODES)
            h_neigh = jnp.where(deg[:, None] > 0, summed / jnp.maximum(deg, 1.0)[:, None], 0.0)
            return x @ W_self + h_neigh @ W_neigh + b
        key = jax.random.key(seed)
        ks = jax.random.split(key, 8)
        x = jax.random.normal(ks[0], (N_NODES, IN_F), dtype=jnp.float32)
        src = jax.random.randint(ks[1], (N_EDGES,), 0, N_NODES, dtype=jnp.int32)
        dst = jax.random.randint(ks[2], (N_EDGES,), 0, N_NODES, dtype=jnp.int32)
        s1 = 1.0 / np.sqrt(IN_F)
        s2 = 1.0 / np.sqrt(HID_F)
        W_self1 = jax.random.normal(ks[3], (IN_F, HID_F), dtype=jnp.float32) * s1
        W_neigh1 = jax.random.normal(ks[4], (IN_F, HID_F), dtype=jnp.float32) * s1
        b1 = jnp.zeros((HID_F,), dtype=jnp.float32)
        W_self2 = jax.random.normal(ks[5], (HID_F, OUT_F), dtype=jnp.float32) * s2
        W_neigh2 = jax.random.normal(ks[6], (HID_F, OUT_F), dtype=jnp.float32) * s2
        b2 = jnp.zeros((OUT_F,), dtype=jnp.float32)
        return {'x': x, 'src': src, 'dst': dst, 'W_self1': W_self1, 'W_neigh1': W_neigh1, 'b1': b1, 'W_self2': W_self2, 'W_neigh2': W_neigh2, 'b2': b2}
    _L1_gnn_all = _L1_gnn_setup()
    _L1_gnn_in = {k: v for k, v in _L1_gnn_all.items() if k in ('W_self1', 'W_neigh1', 'b1', 'W_self2', 'W_neigh2', 'b2')}
    del _L1_gnn_all
    return {'x': x, 'src': src, 'dst': dst, 'L0_gnn_w1': _L0_gnn_in['w1'], 'L0_gnn_b1': _L0_gnn_in['b1'], 'L0_gnn_w2': _L0_gnn_in['w2'], 'L0_gnn_b2': _L0_gnn_in['b2'], 'L0_gnn_w3': _L0_gnn_in['w3'], 'L0_gnn_b3': _L0_gnn_in['b3'], 'L0_gnn_w4': _L0_gnn_in['w4'], 'L0_gnn_b4': _L0_gnn_in['b4'], 'L1_gnn_W_self1': _L1_gnn_in['W_self1'], 'L1_gnn_W_neigh1': _L1_gnn_in['W_neigh1'], 'L1_gnn_b1': _L1_gnn_in['b1'], 'L1_gnn_W_self2': _L1_gnn_in['W_self2'], 'L1_gnn_W_neigh2': _L1_gnn_in['W_neigh2'], 'L1_gnn_b2': _L1_gnn_in['b2']}

def reference(x, src, dst, L0_gnn_w1, L0_gnn_b1, L0_gnn_w2, L0_gnn_b2, L0_gnn_w3, L0_gnn_b3, L0_gnn_w4, L0_gnn_b4, L1_gnn_W_self1, L1_gnn_W_neigh1, L1_gnn_b1, L1_gnn_W_self2, L1_gnn_W_neigh2, L1_gnn_b2):
    import jax
    import jax.numpy as jnp

    def _L0_gnn_ref(x, edge_index, w1, b1, w2, b2, w3, b3, w4, b4):
        import jax, jax.numpy as jnp
        import numpy as np
        N_NODES = 100000
        N_EDGES = 25000
        IN_C, HID_C, OUT_C = (128, 256, 128)
        EPS = 0.0

        def _gin_conv(x, src, dst, mlp):
            agg = jax.ops.segment_sum(x[src], dst, num_segments=N_NODES)
            h = (1.0 + EPS) * x + agg
            return mlp(h)
        src, dst = (edge_index[0], edge_index[1])
        mlp1 = lambda h: jax.nn.relu(h @ w1 + b1) @ w2 + b2
        mlp2 = lambda h: jax.nn.relu(h @ w3 + b3) @ w4 + b4
        h = jax.nn.relu(_gin_conv(x, src, dst, mlp1))
        return _gin_conv(h, src, dst, mlp2)

    def _L1_gnn_ref(x, src, dst, W_self1, W_neigh1, b1, W_self2, W_neigh2, b2):
        import jax, jax.numpy as jnp
        import numpy as np
        N_NODES = 100000
        N_EDGES = 25000
        IN_F, HID_F, OUT_F = (128, 256, 128)

        def _sage_conv(x, src, dst, W_self, W_neigh, b):
            msgs = x[src]
            summed = jax.ops.segment_sum(msgs, dst, num_segments=N_NODES)
            deg = jax.ops.segment_sum(jnp.ones((src.shape[0],), x.dtype), dst, num_segments=N_NODES)
            h_neigh = jnp.where(deg[:, None] > 0, summed / jnp.maximum(deg, 1.0)[:, None], 0.0)
            return x @ W_self + h_neigh @ W_neigh + b
        h = _sage_conv(x, src, dst, W_self1, W_neigh1, b1)
        h = jax.nn.relu(h)
        out = _sage_conv(h, src, dst, W_self2, W_neigh2, b2)
        return out
    edge_index = jnp.stack([src, dst])
    h = jnp.maximum(_layernorm(x, axis=-1), 0.0)
    x = x + _L0_gnn_ref(h, edge_index, L0_gnn_w1, L0_gnn_b1, L0_gnn_w2, L0_gnn_b2, L0_gnn_w3, L0_gnn_b3, L0_gnn_w4, L0_gnn_b4)
    h = jnp.maximum(_layernorm(x, axis=-1), 0.0)
    x = x + _L1_gnn_ref(h, src, dst, L1_gnn_W_self1, L1_gnn_W_neigh1, L1_gnn_b1, L1_gnn_W_self2, L1_gnn_W_neigh2, L1_gnn_b2)
    return x

_drawn_inputs = setup_inputs


def setup_inputs(seed=0):
    import zlib

    import numpy as np

    out = dict(_drawn_inputs(seed))
    spreads = {'L1_gnn_b1': (0.0, 0.1), 'L1_gnn_b2': (0.0, 0.1)}
    factors = {'L0_gnn_b1': 8.0, 'L0_gnn_b2': 6.147, 'L0_gnn_b3': 4.022}
    for name, (base, spread) in spreads.items():
        noise = np.random.default_rng([zlib.crc32(name.encode()), seed]).standard_normal(out[name].shape)
        drawn = base * np.exp(spread * noise) if base else spread * noise
        out[name] = jnp.asarray(drawn.astype(out[name].dtype))
    for name, factor in factors.items():
        out[name] = (out[name] * factor).astype(out[name].dtype)
    return out
```

```python
from contextlib import ExitStack

import concourse.bass as bass
from concourse import mybir
from concourse.alu_op_type import AluOpType as ALU

F32 = mybir.dt.float32
F32R = mybir.dt.float32r
I32 = mybir.dt.int32
ACT = mybir.ActivationFunctionType
AX_X, AX_XY = mybir.AxisListType.X, mybir.AxisListType.XY

IN_F, HID = 128, 256
EPS = 1e-5

SUB = 125
PLACES = 4
GROUP = SUB * PLACES
COLS = 128
STATW = IN_F + 2
RING = 4
PICKW = 576
NOWHERE = 1 << 20
GPART = 100
HALVES = 2
SRC_BITS = 17
CODE0 = 84


class Windows:

    def __init__(self, n, step, span):
        self.n, self.step, self.span = n, step, span
        self.nodes = [PLACES * step] * (n - 1) + [GROUP - PLACES * step * (n - 1)]
        assert n * PLACES * span <= PICKW
        assert step % 2 == 0 and span % 2 == 0


BY_EDGE = Windows(3, 42, 42)
BY_NODE = Windows(4, 30, 36)


def gnn_program(nc, x, src, dst, w1, b1, w2, b2, w3, b3, w4, b4, ws1, wn1, c1, ws2, wn2, c2, out):
    N, E = x.shape[0], src.shape[0]
    G = N // GROUP
    W = BY_EDGE.n
    T, TG = G * W, HALVES * W
    ER = E // SUB
    EPP = E // GPART
    RPP = EPP // SUB
    NOBODY = PLACES * BY_EDGE.step
    assert N == G * GROUP and G == HALVES * GPART and E == ER * SUB and EPP == RPP * SUB and G % (2 * RING) == 0
    PACK = 1 << SRC_BITS

    h1_rows = nc.dram_tensor("h1_rows", (N, HID), F32).ap()
    x1_rows = nc.dram_tensor("x1_rows", (N, STATW), F32).ap()
    z_rows = nc.dram_tensor("z_rows", (N, IN_F), F32).ap()
    part_rows = nc.dram_tensor("part_rows", (N, IN_F), F32).ap()
    sum_rows = nc.dram_tensor("sum_rows", (N, HID), F32).ap()

    def grouped(t):
        return t.rearrange("(g p j) f -> g p j f", p=SUB, j=PLACES)

    ctx = ExitStack()
    with ctx:
        def sb(name, shape, dt=F32, where=ctx):
            return where.enter_context(nc.sbuf_tensor(name, shape, dt))

        sems = {}

        def sem(name):
            if name not in sems:
                sems[name] = ctx.enter_context(nc.semaphore(name))
            return sems[name]

        def wait(eng, s, v):
            if isinstance(v, int) and v <= 0:
                return
            eng.wait_ge(s, v)

        idx_all = sb("idx_all", [128, G * BY_NODE.n], I32)
        loc_all = sb("loc_all", [128, G * BY_NODE.n])
        wgt_all = sb("wgt_all", [128, G * BY_NODE.n])
        ident = sb("ident", [128, 128])
        iota_cols = sb("iota_cols", [128, PLACES * BY_EDGE.span])
        whole = sb("whole", [128, 1], I32)
        ones_r = sb("ones_r", [128, GROUP], F32R)
        eps_col = sb("eps_col", [128, 1])

        W_IN = {"w1": w1, "ws1": ws1, "wn1": wn1}
        W_HID = {"w2": w2, "w3": w3, "w4": w4}
        wf, wh, wl = {}, {}, {}
        for n, w in {**W_IN, **W_HID}.items():
            blocks = w.shape[0] // 128
            wf[n] = sb(n + "_f", [128, blocks, w.shape[1]])
            wh[n] = sb(n + "_hi", [128, blocks, w.shape[1]], F32R)
            wl[n] = sb(n + "_lo", [128, blocks, w.shape[1]], F32R)
        wf["wo"] = sb("wo_f", [128, 2, 2 * IN_F])
        wh["wo"] = sb("wo_hi", [128, 2, 2 * IN_F], F32R)
        wl["wo"] = sb("wo_lo", [128, 2, 2 * IN_F], F32R)

        bias_col = {n: sb(n + "_col", [128, b.shape[0] // 128])
                    for n, b in (("b1", b1), ("b3", b3), ("b4", b4), ("c1", c1), ("c2", c2))}
        bias_r = sb("bias_r", [128, HID], F32R)

        rows = [sb(f"rows{q}", [128, PLACES, HID]) for q in range(RING)]
        idx_ring = [sb(f"idx_ring{q}", [128, PLACES], I32) for q in range(RING)]
        pick = [sb(f"pick{q}", [128, PICKW]) for q in range(RING)]

        banks = [ctx.enter_context(nc.psum_tensor(f"bank{i}", [128, 1024], F32)) for i in range(4)]

        def places(ps, b, used=SUB):
            return ps[:, 512 * b:512 * (b + 1)].rearrange("p (j c) -> p j c", c=COLS)[:, :, 0:used]

        with ExitStack() as own:
            st = lambda name, shape, dt=F32: sb(name, shape, dt, own)
            ss = sem
            bstage = st("bstage", [2, HID])
            bhi, blo = st("bhi", [2, HID], F32R), st("blo", [2, HID])
            dst_i = st("dst_i", [GPART, EPP], I32)
            edge_of = st("edge_of", [GPART, T], I32)
            edge_f = st("edge_f", [GPART, T])
            dst_f = st("dst_f", [GPART, RPP])
            below = st("below", [GPART, RPP, T])
            first_i, first = st("first_i", [GPART, TG], I32), st("first", [GPART, TG])
            nodes = st("nodes", [GPART, TG])
            row_f, row_i, row2_i = st("row_f", [GPART, TG]), st("row_i", [GPART, TG], I32), st("row2_i", [GPART, TG], I32)
            WIN = 252
            dwin, swin = st("dwin", [GPART, TG, WIN], I32), st("swin", [GPART, TG, WIN], I32)
            va, vb, vc = (st(n, [GPART, TG, WIN]) for n in ("va", "vb", "vc"))
            shift_f, shift_i = st("shift_f", [GPART, TG]), st("shift_i", [GPART, TG], I32)
            bit_i, bit, not_bit = st("bit_i", [GPART, TG], I32), st("bit", [GPART, TG]), st("not_bit", [GPART, TG])
            packed_i = st("packed_i", [GPART, TG, SUB], I32)
            slot_node = st("slot_node", [GPART, TG, SUB])
            held, rank, total = (st(n, [GPART, TG, SUB]) for n in ("held", "rank", "total"))
            same = st("same", [GPART, TG + 1, SUB])
            ones_run = st("ones_run", [GPART, TG * SUB])
            tally, verdict, ones_sq = st("tally", [GPART, 2]), st("verdict", [128, 2]), st("ones_sq", [GPART, 128])
            pk_i = st("pk_i", [128, T], I32)
            nd_i, tmp_i, off_i, p0_i = (st(n, [128, T], I32) for n in ("nd_i", "tmp_i", "off_i", "p0_i"))
            ndf, bad, pf = (st(n, [128, T]) for n in ("ndf", "bad", "pf"))

            loaded = ss("su_loaded")
            wloaded = ss("su_wloaded")
            consts = ss("su_consts")
            dchain = ss("su_dve")
            achain = ss("su_act")
            pchain = ss("su_pool")
            cmp_done = ss("su_cmp")
            cnt_done = ss("su_cnt")
            rows_ready = ss("su_rows_ready")
            win_in = ss("su_win_in")
            sent = ss("su_sent")
            wins_ready = ss("su_wins_ready")
            turned = ss("su_turned")
            hi_done = ss("su_hi")
            tallied, summed = ss("su_tallied"), ss("su_summed")

            ps_cnt, ps_pk, ps_w = banks[0], banks[1], banks[2]
            block = own.enter_context(nc.Block())

            @block.sync
            def _(sp):
                sp.dma_start(dst_i[:], dst.rearrange("(p e) -> p e", p=GPART)).then_inc(loaded, 16)
                for n, w in {**W_IN, **W_HID}.items():
                    sp.dma_start(wf[n][:], w.rearrange("(k p) n -> p k n", p=128)).then_inc(wloaded, 16)
                for k, w in enumerate((ws2, wn2)):
                    sp.dma_start(wf["wo"][:, :, IN_F * k:IN_F * (k + 1)],
                                 w.rearrange("(k p) n -> p k n", p=128)).then_inc(wloaded, 16)

            @block.scalar
            def _(act):
                act.dma_start(bstage[:], b2.rearrange("(o n) -> o n", o=1).broadcast_to([2, HID])).then_inc(wloaded, 16)
                with nc.allow_non_contiguous_dma("a few biases, one per partition"):
                    for n, b in (("b1", b1), ("b3", b3), ("b4", b4), ("c1", c1), ("c2", c2)):
                        act.dma_start(bias_col[n][:].unsqueeze(2), b.rearrange("(k p o) -> p k o", p=128, o=1)).then_inc(wloaded, 16)
                act.wait_ge(wloaded, 16 * (len(W_IN) + len(W_HID) + 2 + 6))
                for n in wf:
                    nc.scalar.activation(wh[n][:], wf[n][:], ACT.Copy)
                nc.scalar.activation(bhi[:], bstage[:], ACT.Copy).then_inc(hi_done, 1)

            @block.gpsimd
            def _(pool):
                for h in range(HALVES):
                    nc.gpsimd.iota(edge_of[:, W * GPART * h:W * GPART * (h + 1)], [[PLACES * BY_EDGE.step, W], [GROUP, GPART]],
                                   base=GROUP * GPART * h, channel_multiplier=0)
                    nc.gpsimd.iota(first_i[:, W * h:W * (h + 1)], [[PLACES * BY_EDGE.step, W]],
                                   base=GROUP * GPART * h, channel_multiplier=GROUP)
                    for w in range(W):
                        nc.gpsimd.memset(nodes[:, W * h + w:W * h + w + 1], float(BY_EDGE.nodes[w]))
                nc.gpsimd.iota(off_i[:], [[0, G], [PLACES * BY_EDGE.step, W]], base=0, channel_multiplier=0)
                nc.gpsimd.iota(p0_i[:], [[0, G], [BY_EDGE.step, W]], base=0, channel_multiplier=0)
                nc.gpsimd.iota(iota_cols[:], [[1, PLACES * BY_EDGE.span]], base=0, channel_multiplier=0,
                               allow_small_or_imprecise_dtypes=True)
                nc.gpsimd.memset(ident[:], 0.0).then_inc(pchain, 1)
                pool.wait_ge(pchain, 1)
                nc.gpsimd.affine_select(out=ident[:], in_=ident[:], compare_op=ALU.not_equal, fill=1.0, base=0,
                                        pattern=[[-1, 128]], channel_multiplier=1).then_inc(consts, 1)
                nc.gpsimd.memset(dwin[:], 2 * N)
                nc.gpsimd.memset(swin[:], 0).then_inc(sent, 1)
                for q in range(RING):
                    nc.gpsimd.memset(rows[q][:], 0.0)
                pool.wait_ge(sent, 1)
                pool.wait_ge(rows_ready, 1)
                for win, edges in ((dwin, dst), (swin, src)):
                    table = edges.rearrange("(r c) -> r c", c=SUB)
                    for g in range(TG):
                        for k, ind in enumerate((row_i, row2_i)):
                            nc.gpsimd.indirect_dma_start(
                                out=win[:, g, SUB * k:SUB * (k + 1)], out_offset=None, in_=table,
                                in_offset=bass.IndirectOffsetOnAxis(ap=ind[:, g:g + 1], axis=0),
                                bounds_check=ER - 1, oob_is_err=False).then_inc(win_in, 16)

            @block.tensor
            def _(pe):
                pe.wait_ge(cmp_done, 1)
                for g in range(TG):
                    for r in range(RPP):
                        last = nc.tensor.matmul(ps_cnt[0:GPART, g:g + 1], below[:, r, GPART * g:GPART * (g + 1)],
                                                iota_cols[0:GPART, 1:2], start=(r == 0), stop=(r == RPP - 1))
                last.then_inc(cnt_done, 1)
                pe.wait_ge(tallied, 1)
                nc.tensor.matmul(ps_cnt[:, 512:514], ones_sq[:], tally[:], start=True, stop=True).then_inc(summed, 1)
                pe.wait_ge(wins_ready, 1)
                for ps, win in ((ps_pk, va), (ps_w, total)):
                    for g in range(TG):
                        last = nc.tensor.transpose(ps[0:SUB, 128 * g:128 * g + GPART],
                                                   win[:, g, 0:SUB], ident[0:GPART, 0:GPART])
                last.then_inc(turned, 1)

            @block.vector
            def _(dve):
                count = [0]

                def then(ins):
                    count[0] += 1
                    ins.then_inc(dchain, 1)
                    dve.wait_ge(dchain, count[0])

                V = nc.vector
                V.memset(ones_r[:].bitcast(F32), 1.0)
                V.memset(eps_col[:], EPS)
                V.memset(ones_sq[:], 1.0)
                V.memset(ones_run[:], 1.0)
                V.memset(same[:], 0.0)
                V.memset(bias_r[:].bitcast(F32), 0.0)
                dve.wait_ge(consts, 1)
                V.tensor_copy(edge_f[:], edge_of[:])
                V.tensor_copy(first[:], first_i[:])
                dve.wait_ge(loaded, 16)
                then(V.tensor_copy(dst_f[:], dst_i[:].rearrange("p (r c) -> p r c", c=SUB)[:, :, 0]))
                for r in range(RPP):
                    last = V.tensor_scalar(below[:, r, :], edge_f[:], dst_f[:, r:r + 1], None, ALU.is_gt)
                last.then_inc(cmp_done, 1)
                dve.wait_ge(cnt_done, 1)
                then(V.tensor_scalar(row_f[:], ps_cnt[0:GPART, 0:TG], -1.0, 0.0, ALU.add, ALU.max))
                V.tensor_copy(row_i[:], row_f[:])
                V.tensor_scalar(row2_i[:], row_f[:], 1.0, None, ALU.add).then_inc(rows_ready, 1)
                dve.wait_ge(hi_done, 1)
                for n in wf:
                    V.tensor_tensor(wl[n][:], wf[n][:], wh[n][:].bitcast(F32), ALU.subtract)
                then(V.tensor_tensor(blo[:], bstage[:], bhi[:].bitcast(F32), ALU.subtract))
                then(V.tensor_scalar(bstage[:], bhi[:].bitcast(F32), ident[0:2, 0:1], None, ALU.mult))
                V.scalar_tensor_tensor(out=bias_r[0:2, :], in0=blo[:], scalar=ident[0:2, 1:2], in1=bstage[:],
                                       op0=ALU.mult, op1=ALU.add)
                dve.wait_ge(win_in, 16 * 4 * TG)
                bc = lambda a, w: a.unsqueeze(2).broadcast_to([GPART, TG, w])
                then(V.tensor_tensor(va[:], dwin[:], bc(first[:], WIN), ALU.subtract))
                then(V.tensor_scalar(vb[:], va[:], 0.0, None, ALU.is_ge))
                then(V.tensor_scalar(vc[:, :, 0:SUB], vb[:, :, 0:SUB], -1.0, 1.0, ALU.mult, ALU.add))
                then(V.tensor_reduce(shift_f[:], vc[:, :, 0:SUB], AX_X, ALU.add))
                V.tensor_copy(shift_i[:], shift_f[:])
                then(V.tensor_tensor(vc[:], va[:], bc(nodes[:], WIN), ALU.is_lt))
                then(V.tensor_tensor(vb[:], vb[:], vc[:], ALU.mult))
                then(V.scalar_tensor_tensor(out=vc[:], in0=va[:], scalar=float(-NOBODY), in1=vb[:], op0=ALU.add, op1=ALU.mult))
                then(V.tensor_scalar(va[:], vc[:], float(NOBODY - CODE0), float(PACK), ALU.add, ALU.mult))
                then(V.tensor_tensor(vb[:], va[:], swin[:], ALU.add))
                a, b, width = vb, va, 252
                for k in (6, 5, 4, 3, 2, 1, 0):
                    width = SUB + (1 << k) - 1
                    then(V.tensor_scalar(bit_i[:], shift_i[:], k, 1, ALU.logical_shift_right, ALU.bitwise_and))
                    V.tensor_copy(bit[:], bit_i[:])
                    then(V.tensor_scalar(not_bit[:], bit_i[:], 1.0, None, ALU.is_lt))
                    V.tensor_tensor(vc[:, :, 0:width], a[:, :, 1 << k:(1 << k) + width], bc(bit[:], width), ALU.mult)
                    then(V.tensor_tensor(b[:, :, 0:width], a[:, :, 0:width], bc(not_bit[:], width), ALU.mult))
                    then(V.tensor_tensor(b[:, :, 0:width], vc[:, :, 0:width], b[:, :, 0:width], ALU.add))
                    a, b = b, a
                assert a is va
                then(V.tensor_copy(packed_i[:], va[:, :, 0:SUB]))
                then(V.tensor_scalar(packed_i[:], packed_i[:], SRC_BITS, None, ALU.arith_shift_right))
                then(V.tensor_scalar(slot_node[:], packed_i[:], float(CODE0), None, ALU.add))
                sn = slot_node
                V.tensor_scalar(held[:], sn[:], float(NOBODY), None, ALU.is_lt)
                then(V.tensor_tensor(vb[:, :, 1:SUB], sn[:, :, 1:], sn[:, :, :SUB - 1], ALU.is_lt))
                V.tensor_reduce(tally[:, 0:1], held[:], AX_XY, ALU.add)
                V.tensor_reduce(tally[:, 1:2], vb[:, :, 1:SUB], AX_XY, ALU.add).then_inc(tallied, 1)
                V.tensor_tensor(same[:, 0:TG, 1:SUB], sn[:, :, 1:], sn[:, :, :SUB - 1], ALU.is_equal).then_inc(dchain, 1)
                count[0] += 1
                dve.wait_ge(dchain, count[0])
                n = TG * SUB
                eq, run = same[:].rearrange("p g c -> p (g c)"), rank[:].rearrange("p g c -> p (g c)")
                then(V.tensor_tensor_scan(run[:, 0:n], eq[:, 0:n], ones_run[:, 0:n], 0.0, ALU.mult, ALU.add))
                then(V.tensor_tensor_scan(total[:].rearrange("p g c -> p (g c)")[:, ::-1], eq[:, 1:n + 1][:, ::-1], run[:, 0:n][:, ::-1],
                                          0.0, ALU.mult, ALU.max))
                V.reciprocal(total[:], total[:]).then_inc(wins_ready, 1)
                dve.wait_ge(summed, 1)
                V.tensor_scalar(verdict[:, 0:1], ps_cnt[:, 512:513], float(E), None, ALU.is_equal)
                then(V.tensor_scalar(verdict[:, 1:2], ps_cnt[:, 513:514], 0.0, None, ALU.is_equal))
                V.tensor_tensor(whole[:], verdict[:, 0:1], verdict[:, 1:2], ALU.mult)

                dve.wait_ge(turned, 1)
                P = slice(0, SUB)
                wins = lambda t: t.rearrange("p (h g w) -> p h w g", h=HALVES, w=W)
                turned_in = lambda ps: ps.rearrange("p (h w c) -> p h w c", h=HALVES, c=COLS)[:, :, :, 0:GPART]
                V.tensor_copy(wins(wgt_all[P, 0:T]), turned_in(ps_w[P, 0:TG * COLS]))
                then(V.tensor_copy(wins(pk_i[P]), turned_in(ps_pk[P, 0:TG * COLS])))
                V.tensor_scalar(tmp_i[P], pk_i[P], PACK - 1, None, ALU.bitwise_and)
                then(V.tensor_scalar(nd_i[P], pk_i[P], SRC_BITS, None, ALU.arith_shift_right))
                then(V.tensor_scalar(ndf[P], nd_i[P], float(CODE0), None, ALU.add))
                then(V.tensor_scalar(bad[P], ndf[P], float(NOBODY), None, ALU.is_ge))
                V.scalar_tensor_tensor(out=idx_all[P, 0:T], in0=bad[P], scalar=float(NOWHERE), in1=tmp_i[P], op0=ALU.mult, op1=ALU.add)
                then(V.tensor_tensor(nd_i[P], ndf[P], off_i[P], ALU.add))
                V.tensor_scalar(pk_i[P], nd_i[P], 2, None, ALU.logical_shift_right)
                then(V.tensor_scalar(nd_i[P], nd_i[P], 3, None, ALU.bitwise_and))
                then(V.tensor_tensor(pf[P], pk_i[P], p0_i[P], ALU.subtract))
                then(V.scalar_tensor_tensor(out=ndf[P], in0=nd_i[P], scalar=float(BY_EDGE.span), in1=pf[P], op0=ALU.mult, op1=ALU.add))
                then(V.scalar_tensor_tensor(out=loc_all[P, 0:T], in0=bad[P], scalar=-1000.0, in1=ndf[P], op0=ALU.mult, op1=ALU.add))

        thi = [sb(f"thi{q}", [128, 2, GROUP], F32R) for q in range(2)]
        tlo = [sb(f"tlo{q}", [128, 2, GROUP], F32R) for q in range(2)]
        act_f = [sb(f"act_f{q}", [128, 2, GROUP]) for q in range(2)]
        ahi = [sb(f"ahi{q}", [128, 2, GROUP], F32R) for q in range(2)]
        alo = [sb(f"alo{q}", [128, 2, GROUP], F32R) for q in range(2)]
        P = slice(0, SUB)
        V = nc.vector
        issued = sem("gathers_issued")

        def steps(eng, step, unroll=RING):
            ahead = max(unroll, RING + 1)
            n = (G - RING - ahead) // unroll * unroll
            for k in range(ahead):
                step(k, k)
            with eng.Fori(ahead, ahead + n - unroll + 1, unroll) as i:
                for u in range(unroll):
                    step(i + u, ahead + u)
            for k in range(ahead + n, G + 3):
                step(k, k)

        def product(out_ap, parts, first, last):
            done = None
            for n, (lh, ll, rh, rl) in enumerate(parts):
                nc.tensor.matmul(out_ap, lh, rl, start=(first and n == 0), stop=False)
                nc.tensor.matmul(out_ap, ll, rh, start=False, stop=False)
                done = nc.tensor.matmul(out_ap, lh, rh, start=False, stop=(last and n == len(parts) - 1))
            return done

        def feature_major(ps, w, xs, blocks=2):
            for b in range(blocks):
                o = ps[:, 512 * b:512 * b + GROUP]
                parts = [(wh[n][:, kb, 128 * b:128 * (b + 1)], wl[n][:, kb, 128 * b:128 * (b + 1)], xh, xl)
                         for (n, kb), (xh, xl) in zip(w, xs)]
                done = product(o, parts, True, True)
            return done

        def split_relu(psA, q, bias, done):
            for b in range(2):
                for to in (act_f, ahi):
                    last = nc.scalar.activation(to[q][:, b, :], psA[:, 512 * b:512 * b + GROUP], ACT.Relu, bias=bias_col[bias][:, b:b + 1])
            last.then_inc(done, 1)

        def node_major(out_of, width, wname, hi, lo, bias):
            for j in range(PLACES):
                o = out_of(j)
                if bias is not None:
                    nc.tensor.matmul(o, ones_r[:, 0:SUB], bias[:, 0:width], start=True, stop=False)
                at = lambda t, kb: t[:, kb, SUB * j:SUB * (j + 1)]
                parts = [(at(hi, kb), at(lo, kb), wh[wname][:, kb, 0:width], wl[wname][:, kb, 0:width]) for kb in range(2)]
                done = product(o, parts, bias is None, True)
            return done

        def turn(ps, b, at):
            for j in range(PLACES):
                done = nc.tensor.matmul(ps[:, 512 * b + COLS * j:512 * b + COLS * j + SUB + 1], at(j),
                                        ident[0:SUB + 1, 0:SUB + 1], start=(j == 0), stop=(j == PLACES - 1),
                                        is_transpose=True, skip_group_check=True)
            return done

        def add_windows(win, ps, b, rows_q, pick_q, col, fresh):
            bank = ps[:, 512 * b:512 * (b + 1)].rearrange("p (j c) -> p j c", c=COLS)
            for w in range(win.n):
                done = nc.tensor.matmul(bank[:, :, win.step * w:win.step * w + win.span], rows_q[P, w, col:col + 128],
                                        window_of(win, pick_q, w).rearrange("p (j c) -> p j c", c=win.span),
                                        start=(fresh and w == 0), stop=(w == win.n - 1), skip_group_check=True)
            return done

        def add_split_windows(win, ps, b, hi_q, lo_q, pick_q, col):
            bank = ps[:, 512 * b:512 * (b + 1)].rearrange("p (j c) -> p j c", c=COLS)
            for w in range(win.n):
                for part in (hi_q, lo_q):
                    done = nc.tensor.matmul(bank[:, :, win.step * w:win.step * w + win.span], part[P, w, col:col + 128],
                                            window_of(win, pick_q, w).rearrange("p (j c) -> p j c", c=win.span),
                                            start=False, stop=(w == win.n - 1 and part is lo_q), skip_group_check=True)
            return done

        def window_of(win, pick_q, w):
            width = PLACES * win.span
            return pick_q[P, width * w:width * (w + 1)]

        def gathers(pool, bound, win, k, q, table, width, landed, copied, ring=idx_ring, own=True):
            q_idx = q % len(ring)
            q = q % RING
            if own:
                nc.gpsimd.tensor_copy(ring[q_idx][P, 0:win.n], idx_all[P, bass.ds(k * win.n, win.n)]).then_inc(copied, 1)
            wait(pool, copied, k + 1)
            pool.sem_inc(issued, 1)
            for w in range(win.n):
                nc.gpsimd.indirect_dma_start(
                    out=rows[q][P, w, 0:width], out_offset=None, in_=table,
                    in_offset=bass.IndirectOffsetOnAxis(ap=ring[q_idx][P, w:w + 1], axis=0),
                    bounds_check=bound, oob_is_err=False).then_inc(landed[q], 16)

        def when(eng, want):
            return eng.If(eng.value_load(whole[0:1, 0:1], min_val=0, max_val=1) == want)

        def used2(k, q, n):
            return (k - q) * (n // 2) + n

        def used4(k, q, n):
            return (k - q) * (n // RING) + n

        def phase1(win, table, width, edges):
            phase, tag = "p1_", f"p1{"ge"[edges]}_"
            with ExitStack() as own:
                st = lambda name, shape, dt=F32: sb(name, shape, dt, own)
                ss = sem
                xo = [st(f"{tag}x{q}", [128, PLACES, IN_F]) for q in range(RING)]
                hs = [st(f"{tag}h{q}", [128, PLACES, HID]) for q in range(2)]
                NS = PLACES + win.n
                stats = [st(f"{tag}stats{q}", [128, NS, 6]) for q in range(2)]
                msum, mdif, msq, var, dev, rstd, mean, nmr = (
                    [st(f"{tag}{n}{q}", [128, NS]) for q in range(2)]
                    for n in ("msum", "mdif", "msq", "var", "dev", "rstd", "mean", "nmr"))
                locs = [st(f"{tag}locs{q}", [128, PLACES]) for q in range(2)]
                x_in = [ss(f"{phase}x_in{q}") for q in range(RING)]
                r_in = [ss(f"{phase}r_in{q}") for q in range(RING)]
                h_out = [ss(f"{phase}h_out{q}") for q in range(2)]
                copied = ss(f"{phase}idx_copied")
                s_var, s_dev, s_norm = ss(f"{phase}var"), ss(f"{phase}dev"), ss(f"{phase}norm")
                s_prep, s_own = ss(f"{phase}prep"), ss(f"{phase}own")
                s_T, s_thi, s_tlo = ss(f"{phase}T"), ss(f"{phase}thi"), ss(f"{phase}tlo")
                s_A, s_ahi, s_alo = ss(f"{phase}A"), ss(f"{phase}ahi"), ss(f"{phase}alo")
                s_H, s_hs = ss(f"{phase}H"), ss(f"{phase}hs")
                s_dve, s_zero = ss(f"{phase}dve"), ss(f"{phase}zero")
                psT = [banks[0], banks[1]]
                psA, psH = banks[2], banks[3]
                xg, hg = grouped(x), grouped(h1_rows)
                block = own.enter_context(nc.Block())

                @block.sync
                def _(sp):
                  with when(sp, edges):
                    def load(k, q):
                        sp.dma_start(xo[q][P], xg[k]).then_inc(x_in[q], 16)

                    def step(k, n):
                        q = (n - 3) % 2
                        if n + RING < G:
                            sp.wait_ge(s_T, k + 1)
                            load(k + RING, n % RING)
                        if n >= 3:
                            sp.wait_ge(s_hs, k - 2)
                            sp.dma_start(hg[k - 3], hs[q][P]).then_inc(h_out[q], 16)
                    sp.wait_ge(s_zero, 1)
                    for q in range(RING):
                        load(q, q)
                    steps(sp, step)
                    for q in range(2):
                        sp.wait_ge(h_out[q], 16 * (G // 2))

                @block.gpsimd
                def _(pool):
                  with when(pool, edges):
                    bound = pool.to_reg(N - 1)

                    def step(k, n):
                        if n + RING < G:
                            pool.wait_ge(s_T, k + 1)
                            gathers(pool, bound, win, k + RING, n % RING, table, width, r_in, copied)
                    for q in range(RING):
                        gathers(pool, bound, win, q, q, table, width, r_in, copied)
                    steps(pool, step)
                    for q in range(RING):
                        pool.wait_ge(r_in[q], 16 * win.n * (G // RING))

                @block.vector
                def _(dve):
                  with when(dve, edges):
                    CH = 4

                    def by(factor):
                        return (factor, ALU.is_equal, ALU.mult) if edges else (None, ALU.is_equal)

                    def prepare_a(k, q, r):
                        dve.wait_ge(x_in[r], used4(k, r, 16))
                        for j in range(PLACES):
                            V.bn_stats(stats[q][P, j, :], xo[r][P, j, :])
                        dve.wait_ge(r_in[r], used4(k, r, 16 * win.n))
                        for j in range(win.n):
                            last = V.bn_stats(stats[q][P, PLACES + j, :], rows[r][P, j, 0:IN_F])
                        last.then_inc(s_dve, 1)

                    def prepare_b(k, q, r):
                        s = stats[q]
                        V.tensor_copy(locs[q][P, 0:win.n], loc_all[P, bass.ds(k * win.n, win.n)])
                        dve.wait_ge(s_dve, k * CH + 1)
                        V.tensor_tensor(mdif[q][P], s[P, :, 1], s[P, :, 4], ALU.subtract)
                        V.tensor_tensor(msum[q][P], s[P, :, 1], s[P, :, 4], ALU.add)
                        V.tensor_tensor(var[q][P], s[P, :, 2], s[P, :, 5], ALU.add).then_inc(s_dve, 1)
                        dve.wait_ge(s_dve, k * CH + 2)
                        V.tensor_tensor(msq[q][P], mdif[q][P], mdif[q][P], ALU.mult)
                        V.tensor_scalar(mean[q][P], msum[q][P], 0.5, None, ALU.mult).then_inc(s_dve, 1)
                        dve.wait_ge(s_dve, k * CH + 3)
                        V.scalar_tensor_tensor(out=var[q][P], in0=msq[q][P], scalar=IN_F / 4.0, in1=var[q][P],
                                               op0=ALU.mult, op1=ALU.add).then_inc(s_var, 1)
                        for j in range(win.n if edges else 0):
                            V.tensor_scalar(rows[r][P, j, 0:IN_F], rows[r][P, j, 0:IN_F], mean[q][P, PLACES + j:PLACES + j + 1],
                                            0.0, ALU.subtract, ALU.max)

                    def prepare_c(k, q, r):
                        dve.wait_ge(s_dev, k + 1)
                        V.reciprocal(rstd[q][P], dev[q][P]).then_inc(s_dve, 1)

                    def prepare_d(k, q, r):
                        dve.wait_ge(s_dve, k * CH + 4)
                        V.scalar_tensor_tensor(out=nmr[q][P], in0=mean[q][P], scalar=-1.0, in1=rstd[q][P],
                                               op0=ALU.mult, op1=ALU.mult).then_inc(s_norm, 1)
                        for j in range(win.n):
                            last = V.tensor_scalar(window_of(win, pick[r], j), iota_cols[P, 0:PLACES * win.span], locs[q][P, j:j + 1],
                                                   *by(rstd[q][P, PLACES + j:PLACES + j + 1]))
                        last.then_inc(s_prep, 1)

                    def step(k, n):
                        q = n % 2
                        if n + 2 < G:
                            prepare_a(k + 2, q, (n + 2) % RING)
                        if n < G:
                            dve.wait_ge(s_thi, k + 1)
                            wait(dve, s_A, k - 1)
                            V.tensor_tensor(tlo[q][:, 0, :].rearrange("p (j c) -> p j c", c=SUB), places(psT[q], 0),
                                            thi[q][:, 0, :].bitcast(F32).rearrange("p (j c) -> p j c", c=SUB),
                                            ALU.subtract).then_inc(s_tlo, 1)
                        if n + 2 < G:
                            prepare_b(k + 2, q, (n + 2) % RING)
                            prepare_c(k + 2, q, (n + 2) % RING)
                        if 1 <= n <= G:
                            dve.wait_ge(s_ahi, k)
                            wait(dve, s_H, k - 2)
                            V.tensor_tensor(alo[1 - q][:], act_f[1 - q][:], ahi[1 - q][:].bitcast(F32), ALU.subtract).then_inc(s_alo, 1)
                        if n + 2 < G:
                            wait(dve, s_T, k - 1)
                            prepare_d(k + 2, q, (n + 2) % RING)
                    for q in range(RING):
                        last = V.memset(xo[q][96:128], 0.0)
                    last.then_inc(s_zero, 1)
                    for q in range(2):
                        prepare_a(q, q, q)
                        prepare_b(q, q, q)
                        prepare_c(q, q, q)
                        prepare_d(q, q, q)
                    steps(dve, step)

                @block.scalar
                def _(act):
                  with when(act, edges):
                    A = nc.scalar.activation

                    def root(k, q):
                        act.wait_ge(s_var, k + 1)
                        A(dev[q][P], var[q][P], ACT.Sqrt, bias=eps_col[P, 0:1], scale=1.0 / IN_F).then_inc(s_dev, 1)

                    def normalise(k, q, r):
                        act.wait_ge(s_norm, k + 1)
                        for j in range(PLACES):
                            last = A(xo[r][P, j, :], xo[r][P, j, :], ACT.Relu, bias=nmr[q][P, j:j + 1], scale=rstd[q][P, j:j + 1])
                        last.then_inc(s_own, 1)

                    def step(k, n):
                        q = n % 2
                        if n >= 3:
                            act.wait_ge(s_H, k - 2)
                            if n >= 5:
                                act.wait_ge(h_out[1 - q], used2(k - 5, 1 - q, 16))
                            A(hs[1 - q][P].rearrange("p j f -> p (j f)"), psH[P], ACT.Relu).then_inc(s_hs, 1)
                        if n < G:
                            act.wait_ge(s_T, k + 1)
                            wait(act, s_A, k - 1)
                            A(thi[q][:, 0, :].rearrange("p (j c) -> p j c", c=SUB), places(psT[q], 0), ACT.Copy).then_inc(s_thi, 1)
                        if n + 1 < G:
                            normalise(k + 1, 1 - q, (n + 1) % RING)
                        if 1 <= n <= G:
                            act.wait_ge(s_A, k)
                            wait(act, s_H, k - 2)
                            split_relu(psA, 1 - q, "b1", s_ahi)
                        if n + 2 < G:
                            root(k + 2, q)
                    for q in range(2):
                        root(q, q)
                    normalise(0, 0, 0)
                    steps(act, step)

                @block.tensor
                def _(pe):
                  with when(pe, edges):
                    def step(k, n):
                        q = n % 2
                        if n < G:
                            pe.wait_ge(s_own, k + 1)
                            pe.wait_ge(s_prep, k + 1)
                            wait(pe, s_tlo, k - 1)
                            turn(psT[q], 0, lambda j: xo[n % RING][0:SUB + 1, j, :])
                            add_windows(win, psT[q], 0, rows[n % RING], pick[n % RING], 0, False).then_inc(s_T, 1)
                        if 1 <= n <= G:
                            pe.wait_ge(s_tlo, k)
                            wait(pe, s_ahi, k - 1)
                            feature_major(psA, [("w1", 0)], [(thi[1 - q][:, 0, :], tlo[1 - q][:, 0, :])]).then_inc(s_A, 1)
                        if 2 <= n <= G + 1:
                            pe.wait_ge(s_alo, k - 1)
                            wait(pe, s_hs, k - 2)
                            node_major(lambda j: psH[P, HID * j:HID * (j + 1)], HID, "w2", ahi[q], alo[q], bias_r).then_inc(s_H, 1)
                    steps(pe, step)

        def phase2(win, table, width, edges):
            phase, tag = "p2_", f"p2{"ge"[edges]}_"
            with ExitStack() as own:
                st = lambda name, shape, dt=F32: sb(name, shape, dt, own)
                ss = sem
                ho = [st(f"{tag}h{q}", [128, PLACES, HID]) for q in range(RING)]
                xo = [st(f"{tag}x{q}", [128, PLACES, IN_F]) for q in range(RING)]
                xs = [st(f"{tag}x1{q}", [128, PLACES, STATW]) for q in range(2)]
                rhi = [st(f"{tag}rhi{q}", [128, win.n, HID], F32R) for q in range(RING)]
                rlo = [st(f"{tag}rlo{q}", [128, win.n, HID], F32R) for q in range(RING)]
                ones_at = [st(f"{tag}ones_at{q}", [128, PICKW], F32R) for q in range(RING)]
                yt = [st(f"{tag}yt{q}", [128, PLACES, SUB]) for q in range(2)]
                stats = [st(f"{tag}stats{q}", [128, PLACES, 6]) for q in range(2)]
                msum, mdif, msq, var, dev = (
                    [st(f"{tag}{n}{q}", [128, PLACES]) for q in range(2)] for n in ("msum", "mdif", "msq", "var", "dev"))
                locs = [st(f"{tag}locs{q}", [128, PLACES]) for q in range(2)]
                h_in = [ss(f"{phase}h_in{q}") for q in range(RING)]
                x_in = [ss(f"{phase}x_in{q}") for q in range(RING)]
                r_in = [ss(f"{phase}r_in{q}") for q in range(RING)]
                x_out = [ss(f"{phase}x_out{q}") for q in range(2)]
                copied = ss(f"{phase}idx_copied")
                s_rhi, s_rlo = ss(f"{phase}rhi"), ss(f"{phase}rlo")
                s_yt, s_X = ss(f"{phase}yt"), ss(f"{phase}X")
                s_prep, s_locs = ss(f"{phase}prep"), ss(f"{phase}locs")
                s_T, s_thi, s_tlo = ss(f"{phase}T"), ss(f"{phase}thi"), ss(f"{phase}tlo")
                s_A, s_ahi, s_alo = ss(f"{phase}A"), ss(f"{phase}ahi"), ss(f"{phase}alo")
                s_H, s_x1, s_var, s_dev, s_xs = ss(f"{phase}H"), ss(f"{phase}x1"), ss(f"{phase}var"), ss(f"{phase}dev"), ss(f"{phase}xs")
                s_dve, s_zero = ss(f"{phase}dve"), ss(f"{phase}zero")
                psT = [banks[0], banks[1]]
                psA = banks[2]
                psY, psX = banks[3][:, 0:512], banks[3][:, 512:1024]
                xg, hg, x1g = grouped(x), grouped(h1_rows), grouped(x1_rows)
                block = own.enter_context(nc.Block())

                @block.sync
                def _(sp):
                  with when(sp, edges):
                    def step(k, n):
                        q = n % 2
                        if n + RING < G:
                            sp.wait_ge(s_T, k + 1)
                            sp.dma_start(ho[n % RING][P], hg[k + RING]).then_inc(h_in[n % RING], 16)
                        if n >= 3:
                            if n + 1 < G:
                                sp.wait_ge(s_x1, k - 2)
                                sp.dma_start(xo[(n + 1) % RING][P], xg[k + 1]).then_inc(x_in[(n + 1) % RING], 16)
                            sp.wait_ge(s_xs, k - 2)
                            sp.dma_start(x1g[k - 3], xs[1 - q][P]).then_inc(x_out[1 - q], 16)
                    sp.wait_ge(s_zero, 1)
                    for q in range(RING):
                        sp.dma_start(ho[q][P], hg[q]).then_inc(h_in[q], 16)
                    for q in range(RING):
                        sp.dma_start(xo[q][P], xg[q]).then_inc(x_in[q], 16)
                    steps(sp, step)
                    for q in range(2):
                        sp.wait_ge(x_out[q], 16 * (G // 2))

                @block.gpsimd
                def _(pool):
                  with when(pool, edges):
                    bound = pool.to_reg(N - 1)

                    def step(k, n):
                        if n + RING < G:
                            pool.wait_ge(s_T, k + 1)
                            gathers(pool, bound, win, k + RING, n % RING, table, width, r_in, copied)
                    for q in range(RING):
                        gathers(pool, bound, win, q, q, table, width, r_in, copied)
                    steps(pool, step)
                    for q in range(RING):
                        pool.wait_ge(r_in[q], 16 * win.n * (G // RING))

                @block.vector
                def _(dve):
                  with when(dve, edges):
                    CH = 3

                    def place(k, q, r):
                        V.tensor_copy(locs[q][P, 0:win.n], loc_all[P, bass.ds(k * win.n, win.n)]).then_inc(s_locs, 1)

                    def picks(k, q, r):
                        dve.wait_ge(s_locs, k + 1)
                        for j in range(win.n):
                            last = V.tensor_scalar(window_of(win, ones_at[r], j), iota_cols[P, 0:PLACES * win.span],
                                                   locs[q][P, j:j + 1], None, ALU.is_equal)
                        last.then_inc(s_prep, 1)

                    def low(k, r, windows):
                        dve.wait_ge(s_rhi, k + 1)
                        for j in windows:
                            last = V.tensor_tensor(rlo[r][P, j, :], rows[r][P, j, :], rhi[r][P, j, :].bitcast(F32), ALU.subtract)
                        if win.n - 1 in windows:
                            last.then_inc(s_rlo, 1)

                    def step(k, n):
                        q = n % 2
                        o, g, r3 = 1 - q, k - 3, (n - 3) % RING
                        s = stats[o]
                        nxt = (k + 2, q, (n + 2) % RING)
                        if n >= 3:
                            dve.wait_ge(s_X, k - 2)
                            dve.wait_ge(x_in[r3], used4(g, r3, 16))
                            if n >= 5:
                                dve.wait_ge(x_out[o], used2(k - 5, o, 16))
                            V.tensor_tensor(xs[o][P, :, 0:IN_F], psX[P].rearrange("p (j f) -> p j f", f=IN_F), xo[r3][P],
                                            ALU.add).then_inc(s_x1, 1)
                        if n >= 3:
                            dve.wait_ge(s_x1, k - 2)
                            for j in range(PLACES):
                                last = V.bn_stats(s[P, j, :], xs[o][P, j, 0:IN_F])
                            last.then_inc(s_dve, 1)
                        if n + 2 < G:
                            wait(dve, s_T, k - 1)
                            place(*nxt)
                        if n >= 3:
                            dve.wait_ge(s_dve, g * CH + 1)
                            V.tensor_tensor(mdif[o][P], s[P, :, 1], s[P, :, 4], ALU.subtract)
                            V.tensor_tensor(msum[o][P], s[P, :, 1], s[P, :, 4], ALU.add)
                            V.tensor_tensor(var[o][P], s[P, :, 2], s[P, :, 5], ALU.add).then_inc(s_dve, 1)
                        if n + 1 < G:
                            low(k + 1, (n + 1) % RING, range(0, 1))
                        if n >= 3:
                            dve.wait_ge(s_dve, g * CH + 2)
                            V.tensor_tensor(msq[o][P], mdif[o][P], mdif[o][P], ALU.mult)
                            V.tensor_scalar(xs[o][P, :, IN_F], msum[o][P], 0.5, None, ALU.mult).then_inc(s_dve, 1)
                        if n + 1 < G:
                            low(k + 1, (n + 1) % RING, range(1, 2))
                        if n >= 3:
                            dve.wait_ge(s_dve, g * CH + 3)
                            V.scalar_tensor_tensor(out=var[o][P], in0=msq[o][P], scalar=IN_F / 4.0, in1=var[o][P],
                                                   op0=ALU.mult, op1=ALU.add).then_inc(s_var, 1)
                        if n + 1 < G:
                            low(k + 1, (n + 1) % RING, range(2, win.n))
                        if n + 2 < G:
                            picks(*nxt)
                        if n < G:
                            dve.wait_ge(s_thi, k + 1)
                            wait(dve, s_A, k - 1)
                            V.tensor_tensor(tlo[q][:].rearrange("p b (j c) -> p (b j) c", c=SUB),
                                            psT[q][:].rearrange("p (j c) -> p j c", c=COLS)[:, :, 0:SUB],
                                            thi[q][:].bitcast(F32).rearrange("p b (j c) -> p (b j) c", c=SUB),
                                            ALU.subtract).then_inc(s_tlo, 1)
                        if 1 <= n <= G:
                            dve.wait_ge(s_ahi, k)
                            wait(dve, s_H, k - 2)
                            V.tensor_tensor(alo[1 - q][:], act_f[1 - q][:], ahi[1 - q][:].bitcast(F32), ALU.subtract).then_inc(s_alo, 1)
                        if n >= 3:
                            dve.wait_ge(s_dev, k - 2)
                            V.reciprocal(xs[o][P, :, IN_F + 1], dev[o][P]).then_inc(s_xs, 1)
                    for q in range(RING):
                        last = V.memset(ho[q][96:128], 0.0)
                    last.then_inc(s_zero, 1)
                    for q in range(2):
                        place(q, q, q)
                        picks(q, q, q)
                    low(0, 0, range(win.n))
                    steps(dve, step)

                @block.scalar
                def _(act):
                  with when(act, edges):
                    A = nc.scalar.activation

                    def high(k, r):
                        act.wait_ge(r_in[r], used4(k, r, 16 * win.n))
                        A(rhi[r][P], rows[r][P, 0:win.n, :], ACT.Copy).then_inc(s_rhi, 1)

                    def step(k, n):
                        q = n % 2
                        if n >= 3:
                            act.wait_ge(s_H, k - 2)
                            wait(act, s_X, k - 4)
                            A(yt[1 - q][:].rearrange("p j c -> p (j c)"), psY[:, 0:GROUP], ACT.Identity, bias=bias_col["b4"][:, 0:1]).then_inc(s_yt, 1)
                        if n < G:
                            act.wait_ge(s_T, k + 1)
                            wait(act, s_A, k - 1)
                            A(thi[q][:].rearrange("p b (j c) -> p (b j) c", c=SUB),
                              psT[q][:].rearrange("p (j c) -> p j c", c=COLS)[:, :, 0:SUB], ACT.Copy).then_inc(s_thi, 1)
                        if n + 2 < G:
                            high(k + 2, (n + 2) % RING)
                        if 1 <= n <= G:
                            act.wait_ge(s_A, k)
                            wait(act, s_H, k - 2)
                            split_relu(psA, 1 - q, "b3", s_ahi)
                        if n >= 3:
                            act.wait_ge(s_var, k - 2)
                            A(dev[1 - q][P], var[1 - q][P], ACT.Sqrt, bias=eps_col[P, 0:1], scale=1.0 / IN_F).then_inc(s_dev, 1)
                    for q in range(2):
                        high(q, q)
                    steps(act, step)

                @block.tensor
                def _(pe):
                  with when(pe, edges):
                    def step(k, n):
                        q = n % 2
                        if n < G:
                            r = n % RING
                            pe.wait_ge(h_in[r], used4(k, r, 16))
                            pe.wait_ge(s_prep, k + 1)
                            wait(pe, s_tlo, k - 1)
                            for b in range(2):
                                turn(psT[q], b, lambda j: ho[r][0:SUB + 1, j, 128 * b:128 * (b + 1)])
                                if b == 0:
                                    pe.wait_ge(s_rlo, k + 1)
                                done = add_split_windows(win, psT[q], b, rhi[r], rlo[r], ones_at[r], 128 * b)
                            done.then_inc(s_T, 1)
                        if n >= 3:
                            pe.wait_ge(s_yt, k - 2)
                            wait(pe, s_x1, k - 3)
                            for j in range(PLACES):
                                done = nc.tensor.matmul(psX[P, IN_F * j:IN_F * (j + 1)], yt[1 - q][:, j, :], ident[:],
                                                        start=(j == 0), stop=(j == PLACES - 1), is_transpose=True, skip_group_check=True)
                            done.then_inc(s_X, 1)
                        if 1 <= n <= G:
                            pe.wait_ge(s_tlo, k)
                            wait(pe, s_ahi, k - 1)
                            feature_major(psA, [("w3", 0), ("w3", 1)],
                                          [(thi[1 - q][:, b, :], tlo[1 - q][:, b, :]) for b in range(2)]).then_inc(s_A, 1)
                        if 2 <= n <= G + 1:
                            pe.wait_ge(s_alo, k - 1)
                            wait(pe, s_yt, k - 2)
                            feature_major(psY, [("w4", 0), ("w4", 1)],
                                          [(ahi[q][:, b, :], alo[q][:, b, :]) for b in range(2)], 1).then_inc(s_H, 1)
                    steps(pe, step)

        def phase3(win, table, width, edges):
            phase, tag = "p3_", f"p3{"ge"[edges]}_"
            with ExitStack() as own:
                st = lambda name, shape, dt=F32: sb(name, shape, dt, own)
                ss = sem
                XR = 2 * RING
                xo = [st(f"{tag}x{q}", [128, PLACES, STATW]) for q in range(XR)]
                hn = [st(f"{tag}hn{q}", [128, PLACES, IN_F]) for q in range(RING)]
                zs = [st(f"{tag}z{q}", [128, PLACES, IN_F]) for q in range(2)]
                os = [st(f"{tag}o{q}", [128, PLACES, IN_F]) for q in range(2)]
                locs, fac = ([st(f"{tag}{n}{q}", [128, PLACES]) for q in range(2)] for n in ("locs", "fac"))
                x_in = [ss(f"{phase}x_in{q}") for q in range(XR)]
                r_in = [ss(f"{phase}r_in{q}") for q in range(RING)]
                z_out = [ss(f"{phase}z_out{q}") for q in range(2)]
                o_out = [ss(f"{phase}o_out{q}") for q in range(2)]
                copied = ss(f"{phase}idx_copied")
                s_prep, s_locs = ss(f"{phase}prep"), ss(f"{phase}locs")
                s_T, s_thi, s_tlo = ss(f"{phase}T"), ss(f"{phase}thi"), ss(f"{phase}tlo")
                s_A, s_ahi, s_alo = ss(f"{phase}A"), ss(f"{phase}ahi"), ss(f"{phase}alo")
                s_dve = ss(f"{phase}dve")
                s_H, s_os, s_zs = ss(f"{phase}H"), ss(f"{phase}os"), ss(f"{phase}zs")
                psT = [banks[0], banks[1]]
                psA, psH = banks[2], banks[3]
                x1g, zg, pg = grouped(x1_rows), grouped(z_rows), grouped(part_rows)
                halves = psH[P].rearrange("p (j s f) -> p s j f", s=2, f=IN_F)
                block = own.enter_context(nc.Block())

                @block.sync
                def _(sp):
                  with when(sp, edges):
                    def step(k, n):
                        q = n % 2
                        if n >= 3:
                            sp.wait_ge(s_os, k - 2)
                            if n + 5 < G:
                                sp.dma_start(xo[(n - 3) % XR][P], x1g[k + 5]).then_inc(x_in[(n - 3) % XR], 16)
                            sp.dma_start(pg[k - 3], os[1 - q][P]).then_inc(o_out[1 - q], 16)
                            sp.wait_ge(s_zs, k - 2)
                            sp.dma_start(zg[k - 3], zs[1 - q][P]).then_inc(z_out[1 - q], 16)
                    for q in range(XR):
                        sp.dma_start(xo[q][P], x1g[q]).then_inc(x_in[q], 16)
                    steps(sp, step, XR)
                    for q in range(2):
                        sp.wait_ge(o_out[q], 16 * (G // 2))
                        sp.wait_ge(z_out[q], 16 * (G // 2))

                @block.gpsimd
                def _(pool):
                  with when(pool, edges):
                    bound = pool.to_reg(N - 1)

                    def step(k, n):
                        if n + RING < G:
                            pool.wait_ge(s_T, k + 1)
                            gathers(pool, bound, win, k + RING, n % RING, table, width, r_in, copied)
                    for q in range(RING):
                        gathers(pool, bound, win, q, q, table, width, r_in, copied)
                    steps(pool, step, XR)
                    for q in range(RING):
                        pool.wait_ge(r_in[q], 16 * win.n * (G // RING))

                @block.vector
                def _(dve):
                  with when(dve, edges):
                    def prepare(k, q, r, x):
                        dve.wait_ge(x_in[x], (k - x) * (16 // XR) + 16)
                        for j in range(PLACES):
                            V.tensor_scalar(hn[r][P, j, :], xo[x][P, j, 0:IN_F], xo[x][P, j, IN_F:IN_F + 1],
                                            xo[x][P, j, IN_F + 1:IN_F + 2], ALU.subtract, ALU.mult)
                        dve.wait_ge(r_in[r], used4(k, r, 16 * win.n))
                        V.tensor_copy(locs[q][P, 0:win.n], loc_all[P, bass.ds(k * win.n, win.n)])
                        if edges:
                            V.tensor_tensor(fac[q][P, 0:win.n], wgt_all[P, bass.ds(k * win.n, win.n)],
                                            rows[r][P, 0:win.n, IN_F + 1], ALU.mult).then_inc(s_locs, 1)
                        else:
                            V.tensor_copy(fac[q][P, 0:win.n], wgt_all[P, bass.ds(k * win.n, win.n)]).then_inc(s_locs, 1)
                        for j in range(win.n if edges else 0):
                            V.tensor_scalar(rows[r][P, j, 0:IN_F], rows[r][P, j, 0:IN_F], rows[r][P, j, IN_F:IN_F + 1],
                                            0.0, ALU.subtract, ALU.max)
                        dve.wait_ge(s_locs, k + 1)
                        for j in range(win.n):
                            last = V.tensor_scalar(window_of(win, pick[r], j), iota_cols[P, 0:PLACES * win.span], locs[q][P, j:j + 1],
                                                   fac[q][P, j:j + 1], ALU.is_equal, ALU.mult)
                        last.then_inc(s_prep, 1)

                    def step(k, n):
                        q = n % 2
                        if n >= 3:
                            dve.wait_ge(s_zs, k - 2)
                            if n >= 5:
                                dve.wait_ge(o_out[1 - q], used2(k - 5, 1 - q, 16))
                            V.tensor_tensor(os[1 - q][P], halves[:, 0], xo[(n - 3) % XR][P, :, 0:IN_F], ALU.add).then_inc(s_os, 1)
                        if n < G:
                            dve.wait_ge(s_thi, k + 1)
                            wait(dve, s_A, k - 1)
                            V.scalar_tensor_tensor(out=tlo[q][:].rearrange("p b (j c) -> p (b j) c", c=SUB),
                                                   in0=psT[q][:].rearrange("p (j c) -> p j c", c=COLS)[:, :, 0:SUB], scalar=0.0,
                                                   in1=thi[q][:].bitcast(F32).rearrange("p b (j c) -> p (b j) c", c=SUB),
                                                   op0=ALU.max, op1=ALU.subtract).then_inc(s_tlo, 1)
                        if n + 2 < G:
                            wait(dve, s_T, k - 1)
                            prepare(k + 2, q, (n + 2) % RING, (n + 2) % XR)
                        if 1 <= n <= G:
                            dve.wait_ge(s_ahi, k)
                            wait(dve, s_H, k - 2)
                            V.tensor_tensor(alo[1 - q][:], act_f[1 - q][:], ahi[1 - q][:].bitcast(F32), ALU.subtract).then_inc(s_alo, 1)
                    for q in range(RING):
                        last = V.memset(hn[q][96:128], 0.0)
                    last.then_inc(s_dve, 1)
                    dve.wait_ge(s_dve, 1)
                    for q in range(2):
                        prepare(q, q, q, q)
                    steps(dve, step, XR)

                @block.scalar
                def _(act):
                  with when(act, edges):
                    A = nc.scalar.activation

                    def step(k, n):
                        q = n % 2
                        if n >= 3:
                            act.wait_ge(s_H, k - 2)
                            if n >= 5:
                                act.wait_ge(z_out[1 - q], used2(k - 5, 1 - q, 16))
                            A(zs[1 - q][P], halves[:, 1], ACT.Copy).then_inc(s_zs, 1)
                        if n < G:
                            act.wait_ge(s_T, k + 1)
                            wait(act, s_A, k - 1)
                            A(thi[q][:].rearrange("p b (j c) -> p (b j) c", c=SUB),
                              psT[q][:].rearrange("p (j c) -> p j c", c=COLS)[:, :, 0:SUB], ACT.Relu).then_inc(s_thi, 1)
                        if 1 <= n <= G:
                            act.wait_ge(s_A, k)
                            wait(act, s_H, k - 2)
                            split_relu(psA, 1 - q, "c1", s_ahi)
                    steps(act, step, XR)

                @block.tensor
                def _(pe):
                  with when(pe, edges):
                    def step(k, n):
                        q = n % 2
                        if n < G:
                            pe.wait_ge(s_prep, k + 1)
                            wait(pe, s_tlo, k - 1)
                            turn(psT[q], 0, lambda j: hn[n % RING][0:SUB + 1, j, :])
                            add_windows(win, psT[q], 1, rows[n % RING], pick[n % RING], 0, True).then_inc(s_T, 1)
                        if 1 <= n <= G:
                            pe.wait_ge(s_tlo, k)
                            wait(pe, s_ahi, k - 1)
                            feature_major(psA, [("ws1", 0), ("wn1", 0)],
                                          [(thi[1 - q][:, b, :], tlo[1 - q][:, b, :]) for b in range(2)]).then_inc(s_A, 1)
                        if 2 <= n <= G + 1:
                            pe.wait_ge(s_alo, k - 1)
                            wait(pe, s_os, k - 2)
                            node_major(lambda j: psH[P, HID * j:HID * (j + 1)], HID, "wo", ahi[q], alo[q], None).then_inc(s_H, 1)
                    steps(pe, step, XR)

        def phase4(win, table, width, edges):
            phase, tag = "p4_", f"p4{"ge"[edges]}_"
            with ExitStack() as own:
                st = lambda name, shape, dt=F32: sb(name, shape, dt, own)
                ss = sem
                po = [st(f"{tag}p{q}", [128, PLACES, IN_F]) for q in range(2)]
                zt = [st(f"{tag}zt{q}", [128, PLACES, COLS]) for q in range(2)]
                os = [st(f"{tag}o{q}", [128, PLACES, IN_F]) for q in range(2)]
                IR = 2 * RING
                indices = [st(f"{tag}indices{q}", [128, PLACES], I32) for q in range(IR)]
                locs = [st(f"{tag}locs{q}", [128, PLACES]) for q in range(2)]
                wgts = [st(f"{tag}wgts{q}", [128, PLACES]) for q in range(2)]
                p_in = [ss(f"{phase}p_in{q}") for q in range(2)]
                r_in = [ss(f"{phase}r_in{q}") for q in range(RING)]
                o_out = [ss(f"{phase}o_out{q}") for q in range(2)]
                copied = ss(f"{phase}idx_copied")
                s_prep, s_locs = ss(f"{phase}prep"), ss(f"{phase}locs")
                s_T, s_zt, s_H, s_os = ss(f"{phase}T"), ss(f"{phase}zt"), ss(f"{phase}H"), ss(f"{phase}os")
                psT, psH = [banks[0], banks[1]], [banks[2], banks[3]]
                pg, og = grouped(part_rows), grouped(out)
                block = own.enter_context(nc.Block())

                @block.sync
                def _(sp):
                  with when(sp, edges):
                    def step(k, n):
                        q = n % 2
                        if 1 <= n <= G:
                            sp.wait_ge(s_os, k)
                            sp.dma_start(og[k - 1], os[1 - q][P]).then_inc(o_out[1 - q], 16)
                            if n + 1 < G:
                                sp.dma_start(po[1 - q][P], pg[k + 1]).then_inc(p_in[1 - q], 16)
                    for q in range(2):
                        sp.dma_start(po[q][P], pg[q]).then_inc(p_in[q], 16)
                    steps(sp, step)
                    for q in range(2):
                        sp.wait_ge(o_out[q], 16 * (G // 2))

                @block.gpsimd
                def _(pool):
                  with when(pool, edges):
                    bound = pool.to_reg(N - 1)

                    def step(k, n):
                        if n + RING < G:
                            pool.wait_ge(s_T, k + 1)
                            gathers(pool, bound, win, k + RING, (n + RING) % IR, table, width, r_in, copied, indices, False)
                    for q in range(RING):
                        gathers(pool, bound, win, q, q, table, width, r_in, copied, indices, False)
                    steps(pool, step, IR)
                    for q in range(RING):
                        pool.wait_ge(r_in[q], 16 * win.n * (G // RING))

                @block.vector
                def _(dve):
                  with when(dve, edges):
                    def index(k, r):
                        V.tensor_copy(indices[r][P, 0:win.n], idx_all[P, bass.ds(k * win.n, win.n)]).then_inc(copied, 1)

                    def prepare(k, q, r):
                        V.tensor_copy(locs[q][P, 0:win.n], loc_all[P, bass.ds(k * win.n, win.n)])
                        V.tensor_copy(wgts[q][P, 0:win.n], wgt_all[P, bass.ds(k * win.n, win.n)]).then_inc(s_locs, 1)
                        dve.wait_ge(s_locs, k + 1)
                        for j in range(win.n):
                            last = V.tensor_scalar(window_of(win, pick[r], j), iota_cols[P, 0:PLACES * win.span], locs[q][P, j:j + 1],
                                                   wgts[q][P, j:j + 1], ALU.is_equal, ALU.mult)
                        last.then_inc(s_prep, 1)

                    def step(k, n):
                        q = n % 2
                        if n + 2 < G:
                            wait(dve, s_T, k - 1)
                            if n + RING + 1 < G:
                                index(k + RING + 1, (n + RING + 1) % IR)
                            prepare(k + 2, q, (n + 2) % RING)
                        if 1 <= n <= G:
                            dve.wait_ge(s_H, k)
                            dve.wait_ge(p_in[1 - q], used2(k - 1, 1 - q, 16))
                            if n >= 3:
                                dve.wait_ge(o_out[1 - q], used2(k - 3, 1 - q, 16))
                            V.tensor_tensor(os[1 - q][P], psH[1 - q][P, 0:512].rearrange("p (j f) -> p j f", f=IN_F),
                                            po[1 - q][P], ALU.add).then_inc(s_os, 1)
                    for q in range(RING + 1):
                        index(q, q)
                    for q in range(2):
                        prepare(q, q, q)
                    steps(dve, step, IR)

                @block.scalar
                def _(act):
                  with when(act, edges):
                    def step(k, n):
                        q = n % 2
                        if n < G:
                            act.wait_ge(s_T, k + 1)
                            wait(act, s_H, k - 1)
                            nc.scalar.activation(zt[q][:, :, 0:SUB], places(psT[q], 0), ACT.Identity, bias=bias_col["c2"][:, 0:1]).then_inc(s_zt, 1)
                    steps(act, step)

                @block.tensor
                def _(pe):
                  with when(pe, edges):
                    def step(k, n):
                        q = n % 2
                        if n < G:
                            pe.wait_ge(r_in[n % RING], used4(k, n % RING, 16 * win.n))
                            pe.wait_ge(s_prep, k + 1)
                            wait(pe, s_zt, k - 1)
                            add_windows(win, psT[q], 0, rows[n % RING], pick[n % RING], 0, True).then_inc(s_T, 1)
                        if 1 <= n <= G:
                            pe.wait_ge(s_zt, k)
                            wait(pe, s_os, k - 2)
                            for j in range(PLACES):
                                done = nc.tensor.matmul(psH[1 - q][P, IN_F * j:IN_F * (j + 1)], zt[1 - q][:, j, 0:SUB], ident[:],
                                                        start=True, stop=True, is_transpose=True)
                            done.then_inc(s_H, 1)
                    steps(pe, step)

        def sum_over_edges(name, table, width, kind):
            with ExitStack() as own:
                st = lambda n, shape, dt=F32: sb(f"{name}_{n}", shape, dt, own)
                ss = lambda n: sem(f"se_{n}")
                zeros = st("zeros", [128, PLACES * HID])
                src_col, dst_col, put_col = (st(n, [128, 1], I32) for n in ("src_col", "dst_col", "put_col"))
                dst_row = st("dst_row", [128, SUB], I32)
                dst_f, again = st("dst_f", [128, 1]), st("again", [128, 1])
                same, earlier, both = st("same", [128, SUB]), st("earlier", [128, SUB]), st("both", [128, SUB])
                got, sums = st("got", [128, HID]), st("sums", [128, HID])
                stat, mv, dev, rstd = st("stat", [128, 6]), st("mv", [128, 2]), st("dev", [128, 1]), st("rstd", [128, 1])
                s_zero, cleared, e_in = ss("zero"), ss("cleared"), ss("e_in")
                r_in, sent = sem(f"{name}_r_in"), sem(f"{name}_sent")
                s_var, s_dev, s_ready, s_prod, s_sums, s_dve = (
                    ss(n) for n in ("var", "dev", "ready", "prod", "sums", "dve"))
                ps = banks[0]
                block = own.enter_context(nc.Block())

                @block.sync
                def _(sp):
                    with when(sp, 0):
                        sp.wait_ge(s_zero, 1)
                        with sp.Fori(0, G, 1) as g:
                            sp.dma_start(sum_rows.rearrange("(g p j) f -> g p (j f)", p=SUB, j=PLACES)[g],
                                         zeros[P]).then_inc(cleared, 16)
                            sp.wait_ge(cleared, g * 16 + 16)
                            sp.sem_inc(issued, 1)

                        def load(c):
                            for col, edge in ((src_col, src), (dst_col, dst)):
                                sp.dma_start(col[P], edge.rearrange("(c p o) -> c p o", p=SUB, o=1)[c]).then_inc(e_in, 16)
                            sp.dma_start(dst_row[P], dst.rearrange("(c o e) -> c o e", o=1, e=SUB)[c]
                                         .broadcast_to([SUB, SUB])).then_inc(e_in, 16)
                        load(0)
                        with sp.Fori(1, ER, 1) as c:
                            sp.wait_ge(sent, c * 16)
                            sp.sem_inc(issued, 1)
                            load(c)

                @block.gpsimd
                def _(pool):
                    with when(pool, 0):
                        nc.gpsimd.memset(zeros[:], 0.0).then_inc(s_zero, 1)
                        nc.gpsimd.memset(got[:], 0.0).then_inc(s_zero, 1)
                        nc.gpsimd.memset(earlier[:], 1.0).then_inc(s_zero, 1)
                        pool.wait_ge(s_zero, 3)
                        nc.gpsimd.affine_select(out=earlier[:], in_=earlier[:], compare_op=ALU.is_gt, fill=0.0, base=0,
                                                pattern=[[-1, SUB]], channel_multiplier=1).then_inc(s_zero, 1)
                        bound = pool.to_reg(N - 1)
                        pool.wait_ge(cleared, 16 * G)
                        with pool.Fori(0, ER, 1) as c:
                            pool.wait_ge(e_in, c * 48 + 48)
                            pool.sem_inc(issued, 1)
                            for to, frm, col, w in ((got, table, src_col, width), (sums, sum_rows, dst_col, HID)):
                                nc.gpsimd.indirect_dma_start(
                                    out=to[P, 0:w], out_offset=None, in_=frm,
                                    in_offset=bass.IndirectOffsetOnAxis(ap=col[P, 0:1], axis=0),
                                    bounds_check=bound, oob_is_err=False).then_inc(r_in, 16)
                            pool.wait_ge(s_sums, c + 1)
                            pool.sem_inc(issued, 1)
                            nc.gpsimd.indirect_dma_start(
                                out=sum_rows, out_offset=bass.IndirectOffsetOnAxis(ap=put_col[P, 0:1], axis=0),
                                in_=sums[P, 0:HID], in_offset=None, bounds_check=bound, oob_is_err=False).then_inc(sent, 16)
                            pool.wait_ge(sent, c * 16 + 16)
                            pool.sem_inc(issued, 1)

                @block.vector
                def _(dve):
                    with when(dve, 0):
                        dve.wait_ge(s_zero, 4)
                        with dve.Fori(0, ER, 1) as c:
                            count = [0]

                            per = {"normalise": 7, "normalised": 5, "as_is": 4}[kind]

                            def then(ins):
                                count[0] += 1
                                assert count[0] <= per
                                ins.then_inc(s_dve, 1)
                                dve.wait_ge(s_dve, c * per + count[0])
                            dve.wait_ge(e_in, c * 48 + 48)
                            then(V.tensor_copy(dst_f[P], dst_col[P]))
                            then(V.tensor_scalar(same[P], dst_row[P], dst_f[P, 0:1], None, ALU.is_equal))
                            then(V.tensor_tensor(both[P], same[P], earlier[P], ALU.mult))
                            then(V.tensor_reduce(again[P], both[P], AX_X, ALU.max))
                            dve.wait_ge(r_in, c * 32 + 32)
                            last = V.scalar_tensor_tensor(out=put_col[P], in0=again[P], scalar=float(NOWHERE), in1=dst_f[P],
                                                          op0=ALU.mult, op1=ALU.add)
                            if kind == "normalise":
                                then(V.bn_stats(stat[P], got[P, 0:IN_F]))
                                V.memset(got[P, IN_F:IN_F + 1], 1.0)
                                V.bn_aggr(mv[P], stat[P]).then_inc(s_var, 1)
                                dve.wait_ge(s_dev, c + 1)
                                then(V.reciprocal(rstd[P], dev[P]))
                                then(V.tensor_scalar(got[P, 0:IN_F], got[P, 0:IN_F], mv[P, 0:1], rstd[P, 0:1], ALU.subtract, ALU.mult))
                                V.tensor_scalar(got[P, 0:IN_F], got[P, 0:IN_F], 0.0, None, ALU.max).then_inc(s_ready, 1)
                            elif kind == "normalised":
                                then(V.tensor_scalar(got[P, 0:IN_F], got[P, 0:IN_F], got[P, IN_F:IN_F + 1],
                                                     got[P, IN_F + 1:IN_F + 2], ALU.subtract, ALU.mult))
                                V.tensor_scalar(got[P, 0:IN_F], got[P, 0:IN_F], 0.0, None, ALU.max).then_inc(s_ready, 1)
                            else:
                                last.then_inc(s_ready, 1)
                            dve.wait_ge(s_prod, c + 1)
                            V.tensor_tensor(sums[P], sums[P], ps[P, 0:HID], ALU.add).then_inc(s_sums, 1)

                @block.scalar
                def _(act):
                    if kind == "normalise":
                        with when(act, 0):
                            with act.Fori(0, ER, 1) as c:
                                act.wait_ge(s_var, c + 1)
                                nc.scalar.activation(dev[P], mv[P, 1:2], ACT.Sqrt, bias=eps_col[P, 0:1]).then_inc(s_dev, 1)

                @block.tensor
                def _(pe):
                    with when(pe, 0):
                        with pe.Fori(0, ER, 1) as c:
                            pe.wait_ge(s_ready, c + 1)
                            nc.tensor.matmul(ps[P, 0:HID], same[P, 0:SUB], got[P], start=True, stop=True).then_inc(s_prod, 1)

            with nc.Block() as block:
                @block.gpsimd
                def _(pool):
                    with when(pool, 0):
                        for s in (s_zero, cleared, e_in, s_var, s_dev, s_ready, s_prod, s_sums, s_dve):
                            pool.sem_clear(s)

        def windows_by_node():
            win = BY_NODE
            T4 = G * win.n
            with ExitStack() as own:
                part_i, place_i, p0 = (sb(f"bn_{n}", [128, T4], I32, own) for n in ("part", "place", "p0"))
                first, ready = sem("bn_first"), sem("bn_ready")
                block = own.enter_context(nc.Block())

                @block.gpsimd
                def _(pool):
                    with when(pool, 0):
                        nc.gpsimd.iota(idx_all[:], [[SUB, T4]], base=0, channel_multiplier=1)
                        nc.gpsimd.iota(part_i[:], [[0, G], [SUB, win.n]], base=0, channel_multiplier=1)
                        nc.gpsimd.iota(p0[:], [[0, G], [win.step, win.n]], base=0, channel_multiplier=0).then_inc(first, 1)

                @block.vector
                def _(dve):
                    with when(dve, 0):
                        dve.wait_ge(first, 1)
                        V.tensor_scalar(place_i[:], part_i[:], 3, None, ALU.bitwise_and).then_inc(ready, 1)
                        dve.wait_ge(ready, 1)
                        V.tensor_scalar(part_i[:], part_i[:], 2, None, ALU.logical_shift_right).then_inc(ready, 1)
                        dve.wait_ge(ready, 2)
                        V.tensor_tensor(part_i[:], part_i[:], p0[:], ALU.subtract).then_inc(ready, 1)
                        dve.wait_ge(ready, 3)
                        V.scalar_tensor_tensor(out=loc_all[:], in0=place_i[:], scalar=float(win.span), in1=part_i[:],
                                               op0=ALU.mult, op1=ALU.add)

        def degrees_by_node():
            with ExitStack() as own:
                deg = sb("dn_deg", [128, G * BY_NODE.n], F32, own)
                landed, ready = sem("dn_landed"), sem("dn_ready")
                block = own.enter_context(nc.Block())

                @block.sync
                def _(sp):
                    with when(sp, 0):
                        with nc.allow_non_contiguous_dma("one column of a table"):
                            sp.dma_start(deg[P].unsqueeze(2), sum_rows.rearrange("(t p) f -> p t f", p=SUB)[:, :, IN_F:IN_F + 1]
                                         ).then_inc(landed, 16)
                        sp.wait_ge(landed, 16)

                @block.vector
                def _(dve):
                    with when(dve, 0):
                        dve.wait_ge(landed, 16)
                        V.tensor_scalar(deg[P], deg[P], 1.0, None, ALU.max).then_inc(ready, 1)
                        dve.wait_ge(ready, 1)
                        V.reciprocal(wgt_all[P], deg[P])

        phase1(BY_EDGE, x, IN_F, 1)
        phase2(BY_EDGE, h1_rows, HID, 1)
        phase3(BY_EDGE, x1_rows, STATW, 1)
        phase4(BY_EDGE, z_rows, IN_F, 1)

        windows_by_node()
        sum_over_edges("se1", x, IN_F, "normalise")
        degrees_by_node()
        phase1(BY_NODE, sum_rows, HID, 0)
        sum_over_edges("se2", h1_rows, HID, "as_is")
        phase2(BY_NODE, sum_rows, HID, 0)
        sum_over_edges("se3", x1_rows, STATW, "normalised")
        phase3(BY_NODE, sum_rows, HID, 0)
        sum_over_edges("se4", z_rows, IN_F, "as_is")
        phase4(BY_NODE, sum_rows, HID, 0)


_INS = ["x", "src", "dst", "L0_gnn_w1", "L0_gnn_b1", "L0_gnn_w2", "L0_gnn_b2", "L0_gnn_w3", "L0_gnn_b3",
        "L0_gnn_w4", "L0_gnn_b4", "L1_gnn_W_self1", "L1_gnn_W_neigh1", "L1_gnn_b1", "L1_gnn_W_self2",
        "L1_gnn_W_neigh2", "L1_gnn_b2"]


def kernel(**inputs):
    import numpy as _np
    import concourse.bacc as _bacc
    from concourse import mybir as _mybir
    from concourse.bass_utils import run_bass_kernel_spmd as _run

    nc = _bacc.Bacc("TRN2", target_bir_lowering=False, num_devices=1)
    arrays, args = {}, []
    for name in _INS:
        a = _np.ascontiguousarray(inputs[name])
        arrays[f"in_{name}_dram"] = a
        args.append(nc.dram_tensor(f"in_{name}_dram", a.shape, _mybir.dt.from_np(a.dtype), kind="ExternalInput").ap())
    shape = inputs["x"].shape
    args.append(nc.dram_tensor("out_0_dram", shape, _mybir.dt.float32, kind="ExternalOutput").ap())
    gnn_program(nc, *args)
    r = _run(nc, [arrays], core_ids=[0])
    return r.results[0]["out_0_dram"]
```
